# Optimizing a Trainium2 kernel written in Bass

```python
import numpy as np
import jax
import jax.numpy as jnp

def _softmax(x, axis=-1):
    return jax.nn.softmax(x, axis=axis)

def _gelu(x):
    return jax.nn.gelu(x, approximate=True)

def _silu(x):
    return jax.nn.silu(x)

def _sigmoid(x):
    return jax.nn.sigmoid(x)

def _layernorm(x, axis=-1, eps=1e-05):
    m = jnp.mean(x, axis=axis, keepdims=True)
    v = jnp.var(x, axis=axis, keepdims=True)
    return (x - m) / jnp.sqrt(v + eps)

def _scatter_add(tgt, idx, src, axis=0):
    return tgt.at[idx].add(src)

def _segment_sum(src, seg, n):
    return jax.ops.segment_sum(src, seg, n)
kernel_name = 'mk_adj_preln_d1_adj_r2_9e448b'

def setup_inputs(seed: int=0):
    np.random.seed(seed)
    _w = jnp.asarray

    def _rec_inputs():
        import jax
        import jax.numpy as jnp
        _gk = jax.random.key(seed)
        x = -0.000929 + 1 * jax.random.normal(jax.random.fold_in(_gk, 1), (8192, 128), jnp.float32)
        _a = jax.random.bernoulli(jax.random.fold_in(_gk, 2), 0.000244141, (8192, 8192))
        _a = jnp.logical_or(_a, jnp.eye(8192, dtype=bool))
        _af = _a.astype(jnp.float32)
        _af = _af * jax.random.uniform(jax.random.fold_in(_gk, 3), (8192, 8192), jnp.float32, 0.05, 1)
        adj = _af
        return (x, adj)
    x, adj = _rec_inputs()

    def _L0_gnn_setup():
        import jax, jax.numpy as jnp
        import numpy as np
        N, IN_DIM, OUT_DIM = (4096, 128, 128)
        key = jax.random.key(seed)
        k1, k2, k3, k4 = jax.random.split(key, 4)
        X = jax.random.normal(k1, (N, IN_DIM), dtype=jnp.float32)
        A = jax.random.uniform(k2, (N, N), dtype=jnp.float32)
        bound = 1.0 / np.sqrt(IN_DIM)
        W = jax.random.uniform(k3, (OUT_DIM, IN_DIM), minval=-bound, maxval=bound, dtype=jnp.float32)
        b = jax.random.uniform(k4, (OUT_DIM,), minval=-bound, maxval=bound, dtype=jnp.float32)
        return {'X': X, 'A': A, 'W': W, 'b': b}
    _L0_gnn_all = _L0_gnn_setup()
    _L0_gnn_in = {k: v for k, v in _L0_gnn_all.items() if k in ('W', 'b')}
    del _L0_gnn_all
    return {'x': x, 'adj': adj, 'L0_gnn_W': _L0_gnn_in['W'], 'L0_gnn_b': _L0_gnn_in['b']}

def reference(x, adj, L0_gnn_W, L0_gnn_b):
    import jax
    import jax.numpy as jnp

    def _L0_gnn_ref(X, A, W, b):
        import jax, jax.numpy as jnp
        import numpy as np
        N, IN_DIM, OUT_DIM = (4096, 128, 128)
        n = A.shape[0]
        A_hat = A + jnp.eye(n, dtype=A.dtype)
        d_inv_sqrt = A_hat.sum(axis=1) ** (-0.5)
        A_norm = d_inv_sqrt[:, None] * A_hat * d_inv_sqrt[None, :]
        H = A_norm @ X
        return H @ W.T + b
    h = jnp.maximum(_layernorm(x, axis=-1), 0.0)
    x = x + _L0_gnn_ref(h, adj, L0_gnn_W, L0_gnn_b)
    return x

_drawn_inputs = setup_inputs


def setup_inputs(seed=0):
    import zlib

    import numpy as np

    out = dict(_drawn_inputs(seed))
    spreads = {}
    factors = {}
    for name, (base, spread) in spreads.items():
        noise = np.random.default_rng([zlib.crc32(name.encode()), seed]).standard_normal(out[name].shape)
        drawn = base * np.exp(spread * noise) if base else spread * noise
        out[name] = jnp.asarray(drawn.astype(out[name].dtype))
    for name, factor in factors.items():
        out[name] = (out[name] * factor).astype(out[name].dtype)
    return out
```

```python
import concourse.bass as bass
from concourse import mybir
from concourse.alu_op_type import AluOpType as ALU
from contextlib import ExitStack

P = 128
D = 128
TILES = 4
STRIP = TILES * P
BAND = 3
SLOTS = 14
BANKS = 6
LAG = 2
EPS = 1e-5


def plan(n_strips):
    loads, steps, number = [], [], {}

    def load(i, j, again):
        number[i, j, again] = len(loads)
        loads.append((i, j, again))

    def product(i, j, again):
        group = i + n_strips * again
        first = (j == i + BAND + 1) if again else (j == 0)
        last = j == n_strips - 1 or (not again and j == i + BAND)
        steps.append(("product", number[i, j, again], group, first, last))

    for s in range(n_strips):
        for j in list(range(s + BAND + 1, n_strips)) + list(range(s, min(s + BAND + 1, n_strips))) + list(range(s)):
            load(s, j, False)
        for j in range(s):
            if j == max(s - LAG, 0):
                steps.append(("row sums", s))
            product(s, j, False)
        if s == 0:
            steps.append(("row sums", s))
        for i in range(max(s - BAND, 0), s + 1):
            product(i, s, False)
    tail = [("output", e) for e in range(BAND + 1)]
    for i in range(n_strips - BAND - 1):
        for j in range(i + BAND + 1, n_strips):
            load(i, j, True)
            product(i, j, True)
            if tail:
                steps.append(tail.pop(0))
        tail.append(("output", BAND + 1 + i))
    steps += tail

    LOAD_US, SUM_US, PRODUCT_US = 2.6, 2.4, 3.5
    used = {step[1] for step in steps if step[0] == "product"}
    landed, freed, holder, slots, before = {}, {}, [None] * SLOTS, [], []
    at, clock = 0, 0.0
    for n, (i, j, again) in enumerate(loads):
        slot = min(range(SLOTS), key=lambda k: -1 if holder[k] is None else freed.get(holder[k], 1e9))
        old = holder[slot]
        assert old is None or old in freed
        slots.append(slot)
        before.append(old)
        holder[slot] = n
        start = max(landed.get(n - 1, 0.0), freed.get(old, 0.0))
        landed[n] = start + LOAD_US
        if n not in used:
            freed[n] = landed[n] + SUM_US
        while at < len(steps):
            kind, what = steps[at][:2]
            if kind == "product":
                if what not in landed:
                    break
                clock = max(clock, landed[what]) + PRODUCT_US
                freed[what] = clock
            elif kind == "row sums":
                if (what + 1) * n_strips - 1 not in landed:
                    break
                clock = max(clock, landed[(what + 1) * n_strips - 1] + 2 * SUM_US)
            at += 1
    return loads, steps, slots, before


def preln_gcn_kernel(nc, x, adj, wT, b, out):
    F32 = mybir.dt.float32
    ACT = mybir.ActivationFunctionType
    NS = x.shape[0] // STRIP
    FIRST_PASS = NS * NS
    RETAKEN = NS - BAND - 1
    loads, steps, slot_of, held_before = plan(NS)

    x_v = x.rearrange("(s p a) d -> s p (a d)", p=P, a=TILES)
    out_v = out.rearrange("(s p a) d -> s p (a d)", p=P, a=TILES)

    sum_step = {}
    for s in range(NS):
        for k in range(NS):
            sum_step[s * NS + k] = s * (NS - 1) + max(k, 1)
    product_step = {}
    for step in steps:
        if step[0] == "product":
            product_step[step[1]] = len(product_step) + 1
    fill = []
    for n, k in enumerate(slot_of):
        fill.append(1 + slot_of[:n].count(k))
    group_end = {}
    for step in steps:
        if step[0] == "product" and step[4]:
            group_end[step[2]] = product_step[step[1]]

    with ExitStack() as ctx:
        def sb(name, shape):
            return ctx.enter_context(nc.sbuf_tensor(name, shape, F32))

        def sem(name):
            return ctx.enter_context(nc.semaphore(name))

        block_sb = sb("block_sb", [P, SLOTS, TILES, STRIP])
        g_sb = sb("g_sb", [P, NS, TILES, D])
        part_sb = sb("part_sb", [P, RETAKEN, STRIP])
        acc_sb = sb("acc_sb", [P, TILES * STRIP])
        half_sb = sb("half_sb", [P, 2 * STRIP])
        fold_sb = sb("fold_sb", [P, 2, STRIP])
        ht_sb = sb("ht_sb", [P, 2, STRIP])
        y_sb = sb("y_sb", [P, 2, TILES, D])
        xres_sb = sb("xres_sb", [P, 2, TILES, D])
        scratch_sb = sb("scratch_sb", [P, D])
        wT_sb = sb("wT_sb", [P, D])
        bias_sb = sb("bias_sb", [P, D])
        ident_sb = sb("ident_sb", [P, P])
        ones_sb = sb("ones_sb", [P, 1])
        power_sb = sb("power_sb", [P, TILES])
        sum_sb = sb("sum_sb", [P, NS, TILES])
        negmean_sb = sb("negmean_sb", [P, NS, TILES])
        square_sb = sb("square_sb", [P, NS, TILES])
        var_sb = sb("var_sb", [P, NS, TILES])
        rstd_sb = sb("rstd_sb", [P, NS, TILES])
        shift_sb = sb("shift_sb", [P, NS, TILES])
        rows_sb = sb("rows_sb", [P, NS, TILES])
        dinv_sb = sb("dinv_sb", [P, NS, TILES])

        h_ps = [ctx.enter_context(nc.psum_tensor(f"h_ps{k}", [P, STRIP], F32)) for k in range(BANKS)]
        rows_ps = ctx.enter_context(nc.psum_tensor("rows_ps", [P, 512], F32))
        y_ps = ctx.enter_context(nc.psum_tensor("y_ps", [P, TILES, D], F32))

        block_loaded = [sem(f"block_loaded{k}") for k in range(SLOTS)]
        x_loaded = [sem(f"x_loaded{s}") for s in range(NS)]
        weights_loaded = sem("weights_loaded")
        bias_loaded = sem("bias_loaded")
        xres_loaded = [sem(f"xres_loaded{k}") for k in range(2)]
        ident_zeroed = sem("ident_zeroed")
        ident_ready = sem("ident_ready")
        ones_ready = sem("ones_ready")
        power_ready = sem("power_ready")
        ln_summed = sem("ln_summed")
        ln_centred = sem("ln_centred")
        ln_squared = sem("ln_squared")
        ln_var = sem("ln_var")
        ln_rstd = sem("ln_rstd")
        ln_scale = sem("ln_scale")
        h_ready = sem("h_ready")
        diagonal_added = sem("diagonal_added")
        sums_done = sem("sums_done")
        halves_done = sem("halves_done")
        folded = sem("folded")
        rows_summed = sem("rows_summed")
        rows_copied = sem("rows_copied")
        dinv_ready = sem("dinv_ready")
        g_ready = sem("g_ready")
        products_done = sem("products_done")
        parts_taken = sem("parts_taken")
        wholes_taken = sem("wholes_taken")
        outputs_done = sem("outputs_done")
        outputs_scaled = sem("outputs_scaled")
        xres_biased = sem("xres_biased")
        residual_added = sem("residual_added")
        stored = [sem(f"stored{k}") for k in range(2)]

        block = ctx.enter_context(nc.Block())

        @block.sync
        def _(sp):
            def load_x(s):
                sp.dma_start(g_sb[:, s].rearrange("p a d -> p (a d)"), x_v[s]).then_inc(x_loaded[s], 16)

            load_x(0)
            for n, (i, j, again) in enumerate(loads):
                old = held_before[n]
                if old is not None:
                    if old < FIRST_PASS:
                        sp.wait_ge(sums_done, sum_step[old])
                    if old in product_step:
                        sp.wait_ge(products_done, product_step[old])
                sp.dma_start(block_sb[:, slot_of[n]], adj[i, j]).then_inc(block_loaded[slot_of[n]], 16)
                if n == 1:
                    sp.dma_start(wT_sb[:], wT).then_inc(weights_loaded, 16)
                if n % 2 == 0 and 1 + n // 2 < NS:
                    load_x(1 + n // 2)

        @block.vector
        def _(dve):
            nc.vector.memset(ones_sb[:], 1.0).then_inc(ones_ready, 1)
            halves_seen = 0
            for s in range(NS):
                for k in range(NS):
                    n = s * NS + k
                    tile = block_sb[:, slot_of[n]]
                    dve.wait_ge(block_loaded[slot_of[n]], 16 * fill[n])
                    if loads[n][0] == loads[n][1]:
                        if s == 0:
                            dve.wait_ge(ident_ready, 1)
                        diagonal = tile.rearrange("p a (c q) -> p (a c) q", q=P)[:, 0:TILES * TILES:TILES + 1]
                        nc.vector.tensor_tensor(diagonal, diagonal, ident_sb[:, None, :].to_broadcast([P, TILES, P]),
                                                ALU.add).then_inc(diagonal_added, 1)
                        dve.wait_ge(diagonal_added, s + 1)
                    flat = tile.rearrange("p a i -> p (a i)")
                    if k == 0:
                        continue
                    if k == 1:
                        before = block_sb[:, slot_of[n - 1]].rearrange("p a i -> p (a i)")
                        if s > 0:
                            dve.wait_ge(halves_done, s)
                    else:
                        before = acc_sb[:]
                        dve.wait_ge(sums_done, sum_step[n] - 1)
                    nc.vector.tensor_tensor(acc_sb[:], before, flat, ALU.add).then_inc(sums_done, 1)
                dve.wait_ge(sums_done, (s + 1) * (NS - 1))
                nc.vector.tensor_tensor(half_sb[:], acc_sb[:, 0:2 * STRIP], acc_sb[:, 2 * STRIP:4 * STRIP],
                                        ALU.add).then_inc(halves_done, 1)
                dve.wait_ge(halves_done, s + 1)
                if s >= 2:
                    dve.wait_ge(rows_summed, s - 1)
                nc.vector.tensor_tensor(fold_sb[:, s % 2], half_sb[:, 0:STRIP], half_sb[:, STRIP:2 * STRIP],
                                        ALU.add).then_inc(folded, 1)
                dve.wait_ge(folded, s + 1)
            for i in range(RETAKEN):
                e = BAND + 1 + i
                dve.wait_ge(products_done, group_end[NS + i])
                dve.wait_ge(parts_taken, i + 1)
                dve.wait_ge(outputs_done, e - 1)
                nc.vector.tensor_tensor(ht_sb[:, e % 2], h_ps[(NS + i) % BANKS][:], part_sb[:, i],
                                        ALU.add).then_inc(wholes_taken, 1)

        @block.tensor
        def _(pe):
            pe.wait_ge(ones_ready, 1)
            for step in steps:
                if step[0] == "row sums":
                    s = step[1]
                    pe.wait_ge(folded, s + 1)
                    if s >= 1:
                        pe.wait_ge(rows_copied, s)
                    for a in range(TILES):
                        last = nc.tensor.matmul(rows_ps[:, a:a + 1], fold_sb[:, s % 2, a * P:(a + 1) * P], ones_sb[:],
                                                start=True, stop=True)
                    last.then_inc(rows_summed, 1)
                elif step[0] == "product":
                    _, n, group, first, last_of_group = step
                    i, j, again = loads[n]
                    pe.wait_ge(block_loaded[slot_of[n]], 16 * fill[n])
                    if i == j:
                        pe.wait_ge(diagonal_added, i + 1)
                    pe.wait_ge(g_ready, j + 1)
                    if first and group >= BANKS:
                        old = group - BANKS
                        if old < NS:
                            pe.wait_ge(parts_taken, old + 1)
                        else:
                            pe.wait_ge(wholes_taken, old - NS + 1)
                    for a in range(TILES):
                        mm = nc.tensor.matmul(h_ps[group % BANKS][:], g_sb[:, j, a], block_sb[:, slot_of[n], a],
                                              start=first and a == 0, stop=last_of_group and a == TILES - 1)
                    mm.then_inc(products_done, 1)
                else:
                    e = step[1]
                    if e == 0:
                        pe.wait_ge(weights_loaded, 16)
                    if e <= BAND:
                        pe.wait_ge(parts_taken, RETAKEN + e + 1)
                    else:
                        pe.wait_ge(wholes_taken, e - BAND)
                    if e >= 1:
                        pe.wait_ge(outputs_scaled, e)
                    for a in range(TILES):
                        mm = nc.tensor.matmul(y_ps[:, a], ht_sb[:, e % 2, a * P:(a + 1) * P], wT_sb[:],
                                              start=True, stop=True)
                    mm.then_inc(outputs_done, 1)

        strip_of_output = list(range(RETAKEN, NS)) + list(range(RETAKEN))

        @block.scalar
        def _(act):
            def layernorm_relu(s):
                act.wait_ge(x_loaded[s], 16)
                for a in range(TILES):
                    if s + a > 0:
                        act.wait_ge(ln_summed, s * TILES + a)
                    nc.scalar.activation(scratch_sb[:], g_sb[:, s, a], ACT.Copy,
                                         accum_out=sum_sb[:, s, a:a + 1]).then_inc(ln_summed, 1)
                act.wait_ge(ln_summed, (s + 1) * TILES)
                act.wait_ge(ln_centred, s + 1)
                for a in range(TILES):
                    if s + a > 0:
                        act.wait_ge(ln_squared, s * TILES + a)
                    nc.scalar.activation(scratch_sb[:], g_sb[:, s, a], ACT.Square, bias=negmean_sb[:, s, a:a + 1],
                                         accum_out=square_sb[:, s, a:a + 1]).then_inc(ln_squared, 1)
                act.wait_ge(ln_squared, (s + 1) * TILES)
                act.wait_ge(ln_scale, s + 1)
                for a in range(TILES):
                    nc.scalar.activation(g_sb[:, s, a], g_sb[:, s, a], ACT.Relu, bias=shift_sb[:, s, a:a + 1],
                                         scale=rstd_sb[:, s, a:a + 1]).then_inc(h_ready, 1)

            def take_part(group):
                act.wait_ge(products_done, group_end[group])
                if group < RETAKEN:
                    dst = part_sb[:, group]
                else:
                    e = group - RETAKEN
                    if e >= 2:
                        act.wait_ge(outputs_done, e - 1)
                    dst = ht_sb[:, e % 2]
                nc.scalar.activation(dst, h_ps[group % BANKS][:], ACT.Copy).then_inc(parts_taken, 1)

            def scale_output(e):
                act.wait_ge(outputs_done, e + 1)
                if e >= 2:
                    act.wait_ge(stored[e % 2], 16 * (e // 2))
                for a in range(TILES):
                    ins = nc.scalar.activation(y_sb[:, e % 2, a], y_ps[:, a], ACT.Copy,
                                               scale=dinv_sb[:, strip_of_output[e], a:a + 1])
                ins.then_inc(outputs_scaled, 1)

            layernorm_relu(0)
            for s in range(NS):
                if s + 1 < NS:
                    layernorm_relu(s + 1)
                act.wait_ge(rows_summed, s + 1)
                nc.scalar.activation(rows_sb[:, s], rows_ps[:, 0:TILES], ACT.Copy).then_inc(rows_copied, 1)
                act.wait_ge(dinv_ready, s + 1)
                act.wait_ge(h_ready, (s + 1) * TILES)
                for a in range(TILES):
                    ins = nc.scalar.activation(g_sb[:, s, a], g_sb[:, s, a], ACT.Copy, scale=dinv_sb[:, s, a:a + 1])
                ins.then_inc(g_ready, 1)
                if s >= BAND:
                    take_part(s - BAND)
            for e in range(NS):
                if RETAKEN + e + 1 < NS:
                    take_part(RETAKEN + e + 1)
                scale_output(e)

        @block.gpsimd
        def _(pool):
            nc.gpsimd.memset(ident_sb[:], 0.0).then_inc(ident_zeroed, 1)
            nc.gpsimd.memset(power_sb[:], -0.5).then_inc(power_ready, 1)
            pool.wait_ge(ident_zeroed, 1)
            nc.gpsimd.affine_select(out=ident_sb[:], in_=ident_sb[:], compare_op=ALU.not_equal, fill=1.0, base=0,
                                    pattern=[[-1, P]], channel_multiplier=1).then_inc(ident_ready, 1)
            pool.dma_start(bias_sb[:], b[0:1, :].to_broadcast([P, D])).then_inc(bias_loaded, 16)
            pool.wait_ge(power_ready, 1)

            def layernorm_scale(s):
                pool.wait_ge(ln_summed, (s + 1) * TILES)
                nc.gpsimd.tensor_scalar(negmean_sb[:, s], sum_sb[:, s], -1.0 / D, None, ALU.mult).then_inc(ln_centred, 1)
                pool.wait_ge(ln_squared, (s + 1) * TILES)
                nc.gpsimd.tensor_scalar(var_sb[:, s], square_sb[:, s], 1.0 / D, EPS, ALU.mult, ALU.add).then_inc(ln_var, 1)
                pool.wait_ge(ln_var, s + 1)
                nc.gpsimd.tensor_tensor(rstd_sb[:, s], var_sb[:, s], power_sb[:], ALU.pow).then_inc(ln_rstd, 1)
                pool.wait_ge(ln_rstd, s + 1)
                pool.wait_ge(ln_centred, s + 1)
                nc.gpsimd.tensor_tensor(shift_sb[:, s], negmean_sb[:, s], rstd_sb[:, s], ALU.mult).then_inc(ln_scale, 1)

            layernorm_scale(0)
            for s in range(NS):
                if s + 1 < NS:
                    layernorm_scale(s + 1)
                pool.wait_ge(rows_copied, s + 1)
                nc.gpsimd.tensor_tensor(dinv_sb[:, s], rows_sb[:, s], power_sb[:], ALU.pow).then_inc(dinv_ready, 1)

            def load_residual(e):
                pool.dma_start(xres_sb[:, e % 2].rearrange("p a d -> p (a d)"), x_v[strip_of_output[e]])\
                    .then_inc(xres_loaded[e % 2], 16)

            pool.wait_ge(bias_loaded, 16)
            load_residual(0)
            for e in range(NS):
                if e >= 1:
                    pool.wait_ge(residual_added, e)
                if e + 1 < NS:
                    load_residual(e + 1)
                pool.wait_ge(xres_loaded[e % 2], 16 * (e // 2 + 1))
                nc.gpsimd.tensor_tensor(xres_sb[:, e % 2], xres_sb[:, e % 2],
                                        bias_sb[:, None, :].to_broadcast([P, TILES, D]), ALU.add)\
                    .then_inc(xres_biased, 1)
                pool.wait_ge(xres_biased, e + 1)
                pool.wait_ge(outputs_scaled, e + 1)
                nc.gpsimd.tensor_tensor(y_sb[:, e % 2], y_sb[:, e % 2], xres_sb[:, e % 2], ALU.add)\
                    .then_inc(residual_added, 1)
                pool.wait_ge(residual_added, e + 1)
                pool.dma_start(out_v[strip_of_output[e]], y_sb[:, e % 2].rearrange("p a d -> p (a d)"))\
                    .then_inc(stored[e % 2], 16)
            for k in range(2):
                pool.wait_ge(stored[k], 16 * (NS // 2))


def kernel(x, adj, L0_gnn_W, L0_gnn_b):
    import numpy as np
    import concourse.bacc as bacc
    from concourse.bass_utils import run_bass_kernel_spmd

    n = x.shape[0]
    s = n // STRIP
    blocks = np.asarray(adj).reshape(s, P, TILES, s, P, TILES).transpose(0, 3, 4, 5, 2, 1)
    arrays = {
        "x": np.ascontiguousarray(x),
        "adj": np.ascontiguousarray(blocks).reshape(s, s, P, TILES, STRIP),
        "wT": np.ascontiguousarray(np.asarray(L0_gnn_W).T),
        "b": np.ascontiguousarray(L0_gnn_b).reshape(1, D),
    }
    nc = bacc.Bacc("TRN2", target_bir_lowering=False, num_devices=1)
    args = [nc.dram_tensor(k, v.shape, mybir.dt.from_np(v.dtype), kind="ExternalInput").ap() for k, v in arrays.items()]
    out = nc.dram_tensor("out", (n, D), mybir.dt.float32, kind="ExternalOutput").ap()
    preln_gcn_kernel(nc, *args, out)
    r = run_bass_kernel_spmd(nc, [arrays], core_ids=[0])
    return r.results[0]["out"]
```

```python
import numpy as np
import concourse.bass as bass
from concourse import mybir
from concourse.alu_op_type import AluOpType as ALU
from contextlib import ExitStack

P = 128
D = 128
TILES = 4
STRIP = TILES * P
BAND = 3
SLOTS = 14
BANKS = 6
LAG = 1
EPS = 1e-5

LATE_SLOTS = 5
WHOLE = 4
HALF = TILES // 2
SPLITS = 3
DVE_LATER, PE_LATER, ACT_LATER = 1, 2, 4


def plan(n_strips):
    loads, steps, number = [], [], {}
    order = list(range(4, n_strips - BAND - 1)) + [3, 2, 1, 0]

    def load(i, j, again):
        number[i, j, again] = len(loads)
        loads.append((i, j, again))

    def product(i, j, again):
        group = n_strips + order.index(i) if again else i
        first = (j == i + BAND + 1) if again else (j == 0)
        last = j == n_strips - 1 or (not again and j == i + BAND)
        steps.append(("product", number[i, j, again], group, first, last))

    for s in range(n_strips):
        for j in list(range(s + BAND + 1, n_strips)) + list(range(s, min(s + BAND + 1, n_strips))) + list(range(s)):
            load(s, j, False)
        for j in range(s):
            if j == max(s - LAG, 0):
                steps.append(("row sums", s))
            product(s, j, False)
        if s == 0:
            steps.append(("row sums", s))
        for i in range(max(s - BAND, 0), s + 1):
            product(i, s, False)
    for i in order:
        for j in range(i + BAND + 1, n_strips):
            load(i, j, True)
            product(i, j, True)

    LOAD_US, SUM_US, PRODUCT_US = 2.9, 2.4, 3.5
    used = {step[1] for step in steps if step[0] == "product"}
    landed, freed, holder, slots, before = {}, {}, [None] * SLOTS, [], []
    at, clock = 0, 0.0
    for n, (i, j, again) in enumerate(loads):
        slot = min(range(LATE_SLOTS if again else SLOTS), key=lambda k: -1 if holder[k] is None else freed.get(holder[k], 1e9))
        old = holder[slot]
        assert old is None or old in freed
        slots.append(slot)
        before.append(old)
        holder[slot] = n
        start = max(landed.get(n - 1, 0.0), freed.get(old, 0.0))
        landed[n] = start + LOAD_US
        if n not in used:
            freed[n] = landed[n] + SUM_US
        while at < len(steps):
            kind, what = steps[at][:2]
            if kind == "product":
                if what not in landed:
                    break
                clock = max(clock, landed[what]) + PRODUCT_US
                freed[what] = clock
            elif kind == "row sums":
                if (what + 1) * n_strips - 1 not in landed:
                    break
                clock = max(clock, landed[(what + 1) * n_strips - 1] + 2 * SUM_US)
            at += 1
    return loads, steps, slots, before, order


def preln_gcn_kernel(nc, x, adj, wT, b, out):
    F32 = mybir.dt.float32
    ACT = mybir.ActivationFunctionType
    NS = x.shape[0] // STRIP
    FIRST_PASS = NS * NS
    RETAKEN = NS - BAND - 1
    loads, steps, slot_of, held_before, order = plan(NS)

    x_v = x.rearrange("(s p a) d -> s p (a d)", p=P, a=TILES)
    out_v = out.rearrange("(s p a) d -> s p (a d)", p=P, a=TILES)

    sum_step = {}
    for s in range(NS):
        for k in range(NS):
            sum_step[s * NS + k] = s * (NS - 1) + max(k, 1)
    product_step = {}
    for step in steps:
        if step[0] == "product":
            product_step[step[1]] = len(product_step) + 1
    fill = []
    for n, k in enumerate(slot_of):
        fill.append(1 + slot_of[:n].count(k))
    again_products = [step for step in steps if step[0] == "product" and loads[step[1]][2]]
    early_end = len(product_step) - len(again_products)
    split_half = {}
    for step in again_products[WHOLE:]:
        split_half[step[1]] = 2 * (len(split_half) + 1)

    g_order = []
    for step in again_products[WHOLE:]:
        if loads[step[1]][1] not in g_order:
            g_order.append(loads[step[1]][1])

    def late_steps(later):
        due, made = [[k, e] for k, e in zip(range(BAND + 1), range(BAND + 1))], []
        for at, step in enumerate(again_products):
            made.append(("block", step))
            made += [("strip", e) for when, e in due if when == at]
            due = [d for d in due if d[0] != at]
            if step[4]:
                due.append([at + later, BAND + 1 + step[2] - NS])
        return made + [("strip", e) for _, e in due]

    group_end = {}
    for step in steps:
        if step[0] == "product" and step[4]:
            group_end[step[2]] = split_half.get(step[1], product_step[step[1]])

    with ExitStack() as ctx:
        def sb(name, shape):
            return ctx.enter_context(nc.sbuf_tensor(name, shape, F32))

        def sem(name):
            return ctx.enter_context(nc.semaphore(name))

        block_at = -(-nc.sbuf_base // 32) * 32
        block_sb = sb("block_sb", [P, SLOTS, TILES, STRIP])
        g_sb = sb("g_sb", [P, NS, TILES, D])
        part_sb = sb("part_sb", [P, RETAKEN, STRIP])
        acc_sb = sb("acc_sb", [P, TILES * STRIP])
        half_sb = sb("half_sb", [P, 2 * STRIP])
        fold_sb = sb("fold_sb", [P, 2, STRIP])
        ht_sb = sb("ht_sb", [P, 2, STRIP])
        y_sb = sb("y_sb", [P, 2, TILES, D])
        xres_sb = sb("xres_sb", [P, 2, TILES, D])
        scratch_sb = sb("scratch_sb", [P, D])
        wT_sb = sb("wT_sb", [P, D])
        bias_sb = sb("bias_sb", [P, D])
        ident_sb = sb("ident_sb", [P, P])
        ones_sb = sb("ones_sb", [P, 1])
        power_sb = sb("power_sb", [P, TILES])
        sum_sb = sb("sum_sb", [P, NS, TILES])
        negmean_sb = sb("negmean_sb", [P, NS, TILES])
        square_sb = sb("square_sb", [P, NS, TILES])
        var_sb = sb("var_sb", [P, NS, TILES])
        rstd_sb = sb("rstd_sb", [P, NS, TILES])
        shift_sb = sb("shift_sb", [P, NS, TILES])
        rows_sb = sb("rows_sb", [P, NS, TILES])
        dinv_sb = sb("dinv_sb", [P, NS, TILES])

        F32R = mybir.dt.float32r
        slot_bytes = TILES * STRIP * 4
        space = [block_at + LATE_SLOTS * slot_bytes]

        def reuse(name, shape):
            at = space[0]
            space[0] += 4 * int(np.prod(shape[1:]))
            assert space[0] <= block_at + SLOTS * slot_bytes
            return nc.alloc_sbuf_tensor_at(name, shape, F32R, offset=at)

        LATE_J = NS - BAND - 1
        ghi_sb = reuse("ghi_sb", [P, LATE_J, TILES, D])
        glo_sb = reuse("glo_sb", [P, LATE_J, TILES, D])
        ahi_sb = reuse("ahi_sb", [P, SPLITS, HALF, STRIP])
        alo_sb = reuse("alo_sb", [P, SPLITS, HALF, STRIP])

        h_ps = [ctx.enter_context(nc.psum_tensor(f"h_ps{k}", [P, STRIP], F32)) for k in range(BANKS)]
        rows_ps = ctx.enter_context(nc.psum_tensor("rows_ps", [P, 512], F32))
        y_ps = ctx.enter_context(nc.psum_tensor("y_ps", [P, TILES, D], F32))

        block_loaded = [sem(f"block_loaded{k}") for k in range(SLOTS)]
        x_loaded = [sem(f"x_loaded{s}") for s in range(NS)]
        weights_loaded = sem("weights_loaded")
        bias_loaded = sem("bias_loaded")
        xres_loaded = [sem(f"xres_loaded{k}") for k in range(2)]
        ident_zeroed = sem("ident_zeroed")
        ident_ready = sem("ident_ready")
        ones_ready = sem("ones_ready")
        power_ready = sem("power_ready")
        ln_summed = sem("ln_summed")
        ln_centred = sem("ln_centred")
        ln_squared = sem("ln_squared")
        ln_var = sem("ln_var")
        ln_rstd = sem("ln_rstd")
        ln_scale = sem("ln_scale")
        h_ready = sem("h_ready")
        diagonal_added = sem("diagonal_added")
        sums_done = sem("sums_done")
        halves_done = sem("halves_done")
        folded = sem("folded")
        rows_summed = sem("rows_summed")
        rows_copied = sem("rows_copied")
        dinv_ready = sem("dinv_ready")
        g_ready = sem("g_ready")
        products_done = sem("products_done")
        ghi_ready = sem("ghi_ready")
        glo_ready = sem("glo_ready")
        ahi_ready = sem("ahi_ready")
        alo_ready = sem("alo_ready")
        halves_multiplied = sem("halves_multiplied")
        parts_taken = sem("parts_taken")
        wholes_taken = sem("wholes_taken")
        outputs_done = sem("outputs_done")
        outputs_scaled = sem("outputs_scaled")
        xres_biased = sem("xres_biased")
        residual_added = sem("residual_added")
        stored = [sem(f"stored{k}") for k in range(2)]

        block = ctx.enter_context(nc.Block())

        @block.sync
        def _(sp):
            def load_x(s):
                sp.dma_start(g_sb[:, s].rearrange("p a d -> p (a d)"), x_v[s]).then_inc(x_loaded[s], 16)

            load_x(0)
            for n, (i, j, again) in enumerate(loads):
                old = held_before[n]
                if old is not None:
                    if old < FIRST_PASS:
                        sp.wait_ge(sums_done, sum_step[old])
                    if old in split_half:
                        sp.wait_ge(alo_ready, split_half[old])
                    elif old in product_step:
                        sp.wait_ge(products_done, product_step[old])
                sp.dma_start(block_sb[:, slot_of[n]], adj[i, j]).then_inc(block_loaded[slot_of[n]], 16)
                if n == 1:
                    sp.dma_start(wT_sb[:], wT).then_inc(weights_loaded, 16)
                if n % 2 == 0 and 1 + n // 2 < NS:
                    load_x(1 + n // 2)

        @block.vector
        def _(dve):
            nc.vector.memset(ones_sb[:], 1.0).then_inc(ones_ready, 1)
            for s in range(NS):
                for k in range(NS):
                    n = s * NS + k
                    tile = block_sb[:, slot_of[n]]
                    dve.wait_ge(block_loaded[slot_of[n]], 16 * fill[n])
                    if loads[n][0] == loads[n][1]:
                        if s == 0:
                            dve.wait_ge(ident_ready, 1)
                        diagonal = tile.rearrange("p a (c q) -> p (a c) q", q=P)[:, 0:TILES * TILES:TILES + 1]
                        nc.vector.tensor_tensor(diagonal, diagonal, ident_sb[:, None, :].to_broadcast([P, TILES, P]),
                                                ALU.add).then_inc(diagonal_added, 1)
                        dve.wait_ge(diagonal_added, s + 1)
                    flat = tile.rearrange("p a i -> p (a i)")
                    if k == 0:
                        continue
                    if k == 1:
                        before = block_sb[:, slot_of[n - 1]].rearrange("p a i -> p (a i)")
                        if s > 0:
                            dve.wait_ge(halves_done, s)
                    else:
                        before = acc_sb[:]
                        dve.wait_ge(sums_done, sum_step[n] - 1)
                    nc.vector.tensor_tensor(acc_sb[:], before, flat, ALU.add).then_inc(sums_done, 1)
                dve.wait_ge(sums_done, (s + 1) * (NS - 1))
                nc.vector.tensor_tensor(half_sb[:], acc_sb[:, 0:2 * STRIP], acc_sb[:, 2 * STRIP:4 * STRIP],
                                        ALU.add).then_inc(halves_done, 1)
                dve.wait_ge(halves_done, s + 1)
                if s >= 2:
                    dve.wait_ge(rows_summed, s - 1)
                nc.vector.tensor_tensor(fold_sb[:, s % 2], half_sb[:, 0:STRIP], half_sb[:, STRIP:2 * STRIP],
                                        ALU.add).then_inc(folded, 1)
                dve.wait_ge(folded, s + 1)
            split_j = 0
            for kind, what in late_steps(DVE_LATER):
                if kind == "block":
                    n, j = what[1], loads[what[1]][1]
                    if n not in split_half:
                        continue
                    if j in g_order[split_j:split_j + 1]:
                        split_j += 1
                        dve.wait_ge(ghi_ready, split_j)
                        dve.wait_ge(products_done, early_end)
                        nc.vector.tensor_tensor(glo_sb[:, j - BAND - 1], g_sb[:, j], ghi_sb[:, j - BAND - 1],
                                                ALU.subtract).then_inc(glo_ready, 1)
                    for half in range(2):
                        k = split_half[n] - 2 + half
                        dve.wait_ge(ahi_ready, k + 1)
                        if k >= SPLITS:
                            dve.wait_ge(halves_multiplied, k - SPLITS + 1)
                        nc.vector.tensor_tensor(alo_sb[:, k % SPLITS],
                                                block_sb[:, slot_of[n], half * HALF:(half + 1) * HALF],
                                                ahi_sb[:, k % SPLITS], ALU.subtract).then_inc(alo_ready, 1)
                elif what > BAND:
                    e, group = what, NS + what - BAND - 1
                    dve.wait_ge(halves_multiplied, group_end[group])
                    dve.wait_ge(parts_taken, order[e - BAND - 1] + 1)
                    dve.wait_ge(outputs_done, e - 1)
                    nc.vector.tensor_tensor(ht_sb[:, e % 2], h_ps[group % BANKS][:], part_sb[:, order[e - BAND - 1]],
                                            ALU.add).then_inc(wholes_taken, 1)

        @block.tensor
        def _(pe):
            pe.wait_ge(ones_ready, 1)

            def row_sums(s):
                pe.wait_ge(folded, s + 1)
                if s >= 1:
                    pe.wait_ge(rows_copied, s)
                for a in range(TILES):
                    last = nc.tensor.matmul(rows_ps[:, a:a + 1], fold_sb[:, s % 2, a * P:(a + 1) * P], ones_sb[:],
                                            start=True, stop=True)
                last.then_inc(rows_summed, 1)

            def product(n, group, first, last_of_group):
                i, j, again = loads[n]
                if n not in split_half:
                    pe.wait_ge(block_loaded[slot_of[n]], 16 * fill[n])
                if i == j:
                    pe.wait_ge(diagonal_added, i + 1)
                pe.wait_ge(g_ready, j + 1)
                if first and group >= BANKS:
                    old = group - BANKS
                    if old < NS:
                        pe.wait_ge(parts_taken, old + 1)
                    else:
                        pe.wait_ge(wholes_taken, old - NS + 1)
                bank = h_ps[group % BANKS]
                for a in range(TILES):
                    start, stop = first and a == 0, last_of_group and a == TILES - 1
                    if n not in split_half:
                        mm = nc.tensor.matmul(bank[:], g_sb[:, j, a], block_sb[:, slot_of[n], a], start=start, stop=stop)
                        continue
                    k, jj = split_half[n] - 2 + a // HALF, j - BAND - 1
                    pe.wait_ge(glo_ready, g_order.index(j) + 1)
                    pe.wait_ge(ahi_ready, k + 1)
                    ahi, alo = ahi_sb[:, k % SPLITS, a % HALF], alo_sb[:, k % SPLITS, a % HALF]
                    nc.tensor.matmul(bank[:], ghi_sb[:, jj, a], ahi, start=start, stop=False)
                    nc.tensor.matmul(bank[:], glo_sb[:, jj, a], ahi, start=False, stop=False)
                    pe.wait_ge(alo_ready, k + 1)
                    mm = nc.tensor.matmul(bank[:], ghi_sb[:, jj, a], alo, start=False, stop=stop)
                    if a % HALF == HALF - 1:
                        mm.then_inc(halves_multiplied, 1)
                if n not in split_half:
                    mm.then_inc(products_done, 1)

            def output(e):
                if e == 0:
                    pe.wait_ge(weights_loaded, 16)
                if e <= BAND:
                    pe.wait_ge(parts_taken, RETAKEN + e + 1)
                else:
                    pe.wait_ge(wholes_taken, e - BAND)
                if e >= 1:
                    pe.wait_ge(outputs_scaled, e)
                for a in range(TILES):
                    mm = nc.tensor.matmul(y_ps[:, a], ht_sb[:, e % 2, a * P:(a + 1) * P], wT_sb[:],
                                          start=True, stop=True)
                mm.then_inc(outputs_done, 1)

            for step in steps:
                if step[0] == "row sums":
                    row_sums(step[1])
                elif not loads[step[1]][2]:
                    product(*step[1:])
            for kind, what in late_steps(PE_LATER):
                if kind == "block":
                    product(*what[1:])
                else:
                    output(what)

        strip_of_output = list(range(RETAKEN, NS)) + order

        @block.scalar
        def _(act):
            def layernorm_relu(s):
                act.wait_ge(x_loaded[s], 16)
                for a in range(TILES):
                    if s + a > 0:
                        act.wait_ge(ln_summed, s * TILES + a)
                    nc.scalar.activation(scratch_sb[:], g_sb[:, s, a], ACT.Copy,
                                         accum_out=sum_sb[:, s, a:a + 1]).then_inc(ln_summed, 1)
                act.wait_ge(ln_summed, (s + 1) * TILES)
                act.wait_ge(ln_centred, s + 1)
                for a in range(TILES):
                    if s + a > 0:
                        act.wait_ge(ln_squared, s * TILES + a)
                    nc.scalar.activation(scratch_sb[:], g_sb[:, s, a], ACT.Square, bias=negmean_sb[:, s, a:a + 1],
                                         accum_out=square_sb[:, s, a:a + 1]).then_inc(ln_squared, 1)
                act.wait_ge(ln_squared, (s + 1) * TILES)
                act.wait_ge(ln_scale, s + 1)
                for a in range(TILES):
                    nc.scalar.activation(g_sb[:, s, a], g_sb[:, s, a], ACT.Relu, bias=shift_sb[:, s, a:a + 1],
                                         scale=rstd_sb[:, s, a:a + 1]).then_inc(h_ready, 1)

            def take_part(group):
                act.wait_ge(products_done, group_end[group])
                if group < RETAKEN:
                    dst = part_sb[:, group]
                else:
                    e = group - RETAKEN
                    if e >= 2:
                        act.wait_ge(outputs_done, e - 1)
                    dst = ht_sb[:, e % 2]
                nc.scalar.activation(dst, h_ps[group % BANKS][:], ACT.Copy).then_inc(parts_taken, 1)

            def scale_output(e):
                act.wait_ge(outputs_done, e + 1)
                if e >= 2:
                    act.wait_ge(stored[e % 2], 16 * (e // 2))
                for a in range(TILES):
                    ins = nc.scalar.activation(y_sb[:, e % 2, a], y_ps[:, a], ACT.Copy,
                                               scale=dinv_sb[:, strip_of_output[e], a:a + 1])
                ins.then_inc(outputs_scaled, 1)

            layernorm_relu(0)
            for s in range(NS):
                if s + 1 < NS:
                    layernorm_relu(s + 1)
                act.wait_ge(rows_summed, s + 1)
                nc.scalar.activation(rows_sb[:, s], rows_ps[:, 0:TILES], ACT.Copy).then_inc(rows_copied, 1)
                act.wait_ge(dinv_ready, s + 1)
                act.wait_ge(h_ready, (s + 1) * TILES)
                for a in range(TILES):
                    ins = nc.scalar.activation(g_sb[:, s, a], g_sb[:, s, a], ACT.Copy, scale=dinv_sb[:, s, a:a + 1])
                ins.then_inc(g_ready, 1)
                if s >= BAND:
                    take_part(s - BAND)
            take_part(RETAKEN + 1)
            split_j = 0
            for kind, what in late_steps(ACT_LATER):
                if kind == "block":
                    n, j = what[1], loads[what[1]][1]
                    if n not in split_half:
                        continue
                    if split_half[n] == 2:
                        act.wait_ge(products_done, early_end)
                        act.wait_ge(sums_done, NS * (NS - 1))
                    if j in g_order[split_j:split_j + 1]:
                        split_j += 1
                        act.wait_ge(g_ready, j + 1)
                        nc.scalar.activation(ghi_sb[:, j - BAND - 1], g_sb[:, j], ACT.Copy).then_inc(ghi_ready, 1)
                    act.wait_ge(block_loaded[slot_of[n]], 16 * fill[n])
                    for half in range(2):
                        k = split_half[n] - 2 + half
                        if k >= SPLITS:
                            act.wait_ge(halves_multiplied, k - SPLITS + 1)
                            act.wait_ge(alo_ready, k - SPLITS + 1)
                        nc.scalar.activation(ahi_sb[:, k % SPLITS], block_sb[:, slot_of[n], half * HALF:(half + 1) * HALF],
                                             ACT.Copy).then_inc(ahi_ready, 1)
                else:
                    scale_output(what)
                    if RETAKEN + what + 2 < NS:
                        take_part(RETAKEN + what + 2)

        @block.gpsimd
        def _(pool):
            nc.gpsimd.memset(ident_sb[:], 0.0).then_inc(ident_zeroed, 1)
            nc.gpsimd.memset(power_sb[:], -0.5).then_inc(power_ready, 1)
            pool.wait_ge(ident_zeroed, 1)
            nc.gpsimd.affine_select(out=ident_sb[:], in_=ident_sb[:], compare_op=ALU.not_equal, fill=1.0, base=0,
                                    pattern=[[-1, P]], channel_multiplier=1).then_inc(ident_ready, 1)
            pool.dma_start(bias_sb[:], b[0:1, :].to_broadcast([P, D])).then_inc(bias_loaded, 16)
            pool.wait_ge(power_ready, 1)

            def layernorm_scale(s):
                pool.wait_ge(ln_summed, (s + 1) * TILES)
                nc.gpsimd.tensor_scalar(negmean_sb[:, s], sum_sb[:, s], -1.0 / D, None, ALU.mult).then_inc(ln_centred, 1)
                pool.wait_ge(ln_squared, (s + 1) * TILES)
                nc.gpsimd.tensor_scalar(var_sb[:, s], square_sb[:, s], 1.0 / D, EPS, ALU.mult, ALU.add).then_inc(ln_var, 1)
                pool.wait_ge(ln_var, s + 1)
                nc.gpsimd.tensor_tensor(rstd_sb[:, s], var_sb[:, s], power_sb[:], ALU.pow).then_inc(ln_rstd, 1)
                pool.wait_ge(ln_rstd, s + 1)
                pool.wait_ge(ln_centred, s + 1)
                nc.gpsimd.tensor_tensor(shift_sb[:, s], negmean_sb[:, s], rstd_sb[:, s], ALU.mult).then_inc(ln_scale, 1)

            layernorm_scale(0)
            for s in range(NS):
                if s + 1 < NS:
                    layernorm_scale(s + 1)
                pool.wait_ge(rows_copied, s + 1)
                nc.gpsimd.tensor_tensor(dinv_sb[:, s], rows_sb[:, s], power_sb[:], ALU.pow).then_inc(dinv_ready, 1)

            def load_residual(e):
                pool.dma_start(xres_sb[:, e % 2].rearrange("p a d -> p (a d)"), x_v[strip_of_output[e]])\
                    .then_inc(xres_loaded[e % 2], 16)

            pool.wait_ge(bias_loaded, 16)
            load_residual(0)
            for e in range(NS):
                if e >= 1:
                    pool.wait_ge(residual_added, e)
                if e + 1 < NS:
                    load_residual(e + 1)
                pool.wait_ge(xres_loaded[e % 2], 16 * (e // 2 + 1))
                nc.gpsimd.tensor_tensor(xres_sb[:, e % 2], xres_sb[:, e % 2],
                                        bias_sb[:, None, :].to_broadcast([P, TILES, D]), ALU.add)\
                    .then_inc(xres_biased, 1)
                pool.wait_ge(xres_biased, e + 1)
                pool.wait_ge(outputs_scaled, e + 1)
                nc.gpsimd.tensor_tensor(y_sb[:, e % 2], y_sb[:, e % 2], xres_sb[:, e % 2], ALU.add)\
                    .then_inc(residual_added, 1)
                pool.wait_ge(residual_added, e + 1)
                pool.dma_start(out_v[strip_of_output[e]], y_sb[:, e % 2].rearrange("p a d -> p (a d)"))\
                    .then_inc(stored[e % 2], 16)
            for k in range(2):
                pool.wait_ge(stored[k], 16 * (NS // 2))


def kernel(x, adj, L0_gnn_W, L0_gnn_b):
    import numpy as np
    import concourse.bacc as bacc
    from concourse.bass_utils import run_bass_kernel_spmd

    n = x.shape[0]
    s = n // STRIP
    blocks = np.asarray(adj).reshape(s, P, TILES, s, P, TILES).transpose(0, 3, 4, 5, 2, 1)
    arrays = {
        "x": np.ascontiguousarray(x),
        "adj": np.ascontiguousarray(blocks).reshape(s, s, P, TILES, STRIP),
        "wT": np.ascontiguousarray(np.asarray(L0_gnn_W).T),
        "b": np.ascontiguousarray(L0_gnn_b).reshape(1, D),
    }
    nc = bacc.Bacc("TRN2", target_bir_lowering=False, num_devices=1)
    args = [nc.dram_tensor(k, v.shape, mybir.dt.from_np(v.dtype), kind="ExternalInput").ap() for k, v in arrays.items()]
    out = nc.dram_tensor("out", (n, D), mybir.dt.float32, kind="ExternalOutput").ap()
    preln_gcn_kernel(nc, *args, out)
    r = run_bass_kernel_spmd(nc, [arrays], core_ids=[0])
    return r.results[0]["out"]
```

```python
import numpy as np
import concourse.bass as bass
from concourse import mybir
from concourse.alu_op_type import AluOpType as ALU
from contextlib import ExitStack

P = 128
D = 128
TILES = 4
STRIP = TILES * P
BANKS = 6
LAG = 1
X_AT = 4
EPS = 1e-5

SPLIT_FROM = 9
SPLIT_J = 3
SPLIT_LAG = 1
HALF = TILES // 2
SPLITS = 3
DVE_LATER, PE_LATER, ACT_LATER = 1, 2, 4

LATE_SLOTS, DIGIT_SLOTS, FIRST_DIGIT_SLOTS, STAGE_SLOTS = 7, 4, 2, 3
SLOTS = LATE_SLOTS + DIGIT_SLOTS + FIRST_DIGIT_SLOTS + STAGE_SLOTS
LAST_IN_DIGITS = 15
LAST_IN_STAGE = SPLIT_FROM - 1

BANDS = [5, 4, 4, 4, 4, 3, 3, 2, 2, 2, 1, 1, 1, 1, 1, 1]


def split_columns(s):
    return range(min(SPLIT_J, s - SPLIT_FROM + 2)) if s >= SPLIT_FROM else range(0)


def reach(i, n_strips):
    return min(i + BANDS[i], n_strips - 1)


def guests(n_strips):
    retaken = sum(reach(i, n_strips) < n_strips - 1 for i in range(n_strips))
    parts = [("part", i, reach(i, n_strips) - 1) for i in range(retaken - TILES, 1, -TILES)]
    return parts + [("g", i, i - 3) for i in range(n_strips - TILES, TILES, -TILES)]


def plan(n_strips):
    loads, steps, number, split = [], [], {}, []
    guest_slots = guests(n_strips)
    retaken = sum(reach(i, n_strips) < n_strips - 1 for i in range(n_strips))
    order = list(range(TILES, retaken)) + [3, 2, 1, 0]

    def load(i, j, again):
        number[i, j, again] = len(loads)
        loads.append((i, j, again))

    def product(i, j, again):
        group = n_strips + order.index(i) if again else i
        first = group not in {step[2] for step in steps if step[0] == "product"}
        last = j == (n_strips - 1 if again else reach(i, n_strips))
        steps.append(("product", number[i, j, again], group, first, last))

    for s in range(n_strips):
        kept = reach(s, n_strips)
        left = [j for j in range(s) if j not in split_columns(s)]
        left += split_columns(s)
        for j in list(range(kept + 1, n_strips)) + list(range(s, kept + 1)) + left:
            load(s, j, False)
        for at, j in enumerate(left):
            if at == max(s - LAG, 0):
                steps.append(("row sums", s))
            product(s, j, False)
            if j in split_columns(s):
                split.append(number[s, j, False])
        if s == 0:
            steps.append(("row sums", s))
        for i in range(s + 1):
            if reach(i, n_strips) >= s:
                product(i, s, False)
    for i in order:
        for j in range(reach(i, n_strips) + 1, n_strips):
            load(i, j, True)
            product(i, j, True)
            split.append(number[i, j, True])
    first_again = n_strips * n_strips
    split_after = {}
    for n in split:
        if n < first_again:
            split_after.setdefault(min(n + SPLIT_LAG, first_again - 1), []).append(n)

    LOAD_US, LANDING_US, SUM_US, PRODUCT_US = 2.92, 2.0, 2.4, 3.45
    HIGH_US, LOW_US, THREE_US = 1.0, 1.25, 2.6
    used = {step[1] for step in steps if step[0] == "product"}
    landed, freed, slots, before, split_done, multiplied = {}, {}, [], [], {}, {}
    holder = [None] * (SLOTS + len(guest_slots))
    at, clock, dma, act, dve = 0, 0.0, 0.0, 0.0, 0.0
    last_strip = ([n_strips] * LATE_SLOTS + [LAST_IN_DIGITS] * DIGIT_SLOTS
                  + [LAST_IN_STAGE] * (FIRST_DIGIT_SLOTS + STAGE_SLOTS) + [guest[2] for guest in guest_slots])

    def split_estimate(n):
        nonlocal act, dve
        stage = split.index(n) - SPLITS // 2 - 1
        start = max(landed[n], multiplied[split[stage]] if stage >= 0 else 0.0)
        act = max(act, start) + 2 * HIGH_US
        dve = max(dve, act - HIGH_US) + 2 * LOW_US
        split_done[n] = freed[n] = dve

    for n, (i, j, again) in enumerate(loads):
        leaves = n_strips if again else max(i, j) if n in used else i
        choice = [k for k in reversed(range(len(holder))) if leaves <= last_strip[k]]
        slot = min(choice, key=lambda k: -1 if holder[k] is None else freed.get(holder[k], 1e9))
        old = holder[slot]
        assert old is None or old in freed
        slots.append(slot)
        before.append(old)
        holder[slot] = n
        dma = max(dma, freed.get(old, 0.0)) + LOAD_US
        landed[n] = dma + LANDING_US
        if not again and n % n_strips > 0:
            dve = max(dve, landed[n]) + SUM_US
            for m in range(n - (n % n_strips == 1), n + 1):
                if m not in used:
                    freed[m] = dve
        if again and n in split:
            split_estimate(n)
        else:
            for m in split_after.get(n, []):
                split_estimate(m)
        while at < len(steps):
            kind, what = steps[at][:2]
            if kind == "product":
                if what not in landed or what in split and what not in split_done:
                    break
                if what in split:
                    clock = max(clock + THREE_US, split_done[what] + THREE_US / 2)
                else:
                    clock = max(clock, landed[what]) + PRODUCT_US
                    freed[what] = clock
                multiplied[what] = clock
            elif kind == "row sums":
                if (what + 1) * n_strips - 1 not in landed:
                    break
                clock = max(clock, landed[(what + 1) * n_strips - 1] + 2 * SUM_US)
            at += 1
    return loads, steps, slots, before, order, split, split_after


def preln_gcn_kernel(nc, x, adj, wT, b, out):
    F32 = mybir.dt.float32
    ACT = mybir.ActivationFunctionType
    NS = x.shape[0] // STRIP
    FIRST_PASS = NS * NS
    RETAKEN = sum(reach(i, NS) < NS - 1 for i in range(NS))
    DIRECT = NS - RETAKEN
    LATE_J = reach(0, NS) + 1
    loads, steps, slot_of, held_before, order, split, split_after = plan(NS)

    guest_slots = guests(NS)

    x_v = x.rearrange("(s p a) d -> s p (a d)", p=P, a=TILES)
    out_v = out.rearrange("(s p a) d -> s p (a d)", p=P, a=TILES)

    sum_step = {}
    for s in range(NS):
        for k in range(NS):
            sum_step[s * NS + k] = s * (NS - 1) + max(k, 1)
    split_half = {n: 2 * (k + 1) for k, n in enumerate(split)}
    product_step = {}
    for step in steps:
        if step[0] == "product" and step[1] not in split_half:
            product_step[step[1]] = len(product_step) + 1
    fill = []
    for n, k in enumerate(slot_of):
        fill.append(1 + slot_of[:n].count(k))
    again_products = [step for step in steps if step[0] == "product" and loads[step[1]][2]]
    digits = []
    for n in split:
        if (loads[n][2], loads[n][1]) not in digits:
            digits.append((loads[n][2], loads[n][1]))
    first_late = min(n for n in split if loads[n][2])

    def late_steps(later):
        due, made = [[k, e] for k, e in enumerate(range(DIRECT))], []
        for at, step in enumerate(again_products):
            made.append(("block", step))
            made += [("strip", e) for when, e in due if when == at]
            due = [d for d in due if d[0] != at]
            if step[4]:
                due.append([at + later, DIRECT + step[2] - NS])
        return made + [("strip", e) for _, e in due]

    group_end = {}
    for step in steps:
        if step[0] == "product" and step[4]:
            group_end[step[2]] = step[1]

    with ExitStack() as ctx:
        def sb(name, shape):
            return ctx.enter_context(nc.sbuf_tensor(name, shape, F32))

        def sem(name):
            return ctx.enter_context(nc.semaphore(name))

        block_at = -(-nc.sbuf_base // 32) * 32
        block_sb = sb("block_sb", [P, SLOTS, TILES, STRIP])
        g_at = -(-nc.sbuf_base // 32) * 32
        g_sb = sb("g_sb", [P, NS, TILES, D])
        part_at = -(-nc.sbuf_base // 32) * 32
        part_sb = sb("part_sb", [P, RETAKEN, STRIP])
        acc_at = -(-nc.sbuf_base // 32) * 32
        acc_sb = sb("acc_sb", [P, TILES * STRIP])
        fold_sb = sb("fold_sb", [P, 2, STRIP])
        ht_sb = sb("ht_sb", [P, 2, STRIP])
        y_sb = nc.alloc_sbuf_tensor_at("y_sb", [P, 2, TILES, D], F32, offset=acc_at)
        xres_sb = nc.alloc_sbuf_tensor_at("xres_sb", [P, 2, TILES, D], F32, offset=acc_at + 2 * STRIP * 4)
        guest_sb = [nc.alloc_sbuf_tensor_at(f"guest{k}_sb", [P, TILES, STRIP], F32,
                                            offset={"part": part_at, "g": g_at}[buffer] + first * STRIP * 4)
                    for k, (buffer, first, _) in enumerate(guest_slots)]

        def slot_ap(k):
            return block_sb[:, k] if k < SLOTS else guest_sb[k - SLOTS][:]

        scratch_sb = sb("scratch_sb", [P, D])
        wT_sb = sb("wT_sb", [P, D])
        bias_sb = sb("bias_sb", [P, D])
        ident_sb = sb("ident_sb", [P, P])
        ones_sb = sb("ones_sb", [P, 1])
        power_sb = sb("power_sb", [P, TILES])
        sum_sb = sb("sum_sb", [P, 2, TILES])
        negmean_sb = sb("negmean_sb", [P, 2, TILES])
        square_sb = sb("square_sb", [P, 2, TILES])
        var_sb = sb("var_sb", [P, 2, TILES])
        rstd_sb = sb("rstd_sb", [P, 2, TILES])
        shift_sb = sb("shift_sb", [P, 2, TILES])
        rows_sb = sb("rows_sb", [P, NS, TILES])
        dinv_sb = sb("dinv_sb", [P, NS, TILES])

        F32R = mybir.dt.float32r
        slot_bytes = TILES * STRIP * 4

        def reuse(name, slots, shape, at=0):
            assert at + 4 * int(np.prod(shape[1:])) <= len(slots) * slot_bytes
            return nc.alloc_sbuf_tensor_at(name, shape, F32R, offset=block_at + slots[0] * slot_bytes + at)

        stage_slots = range(SLOTS - STAGE_SLOTS, SLOTS)
        first_digit_slots = range(LATE_SLOTS + DIGIT_SLOTS, SLOTS - STAGE_SLOTS)
        digit_slots = range(LATE_SLOTS, SLOTS - STAGE_SLOTS)
        half_bytes, strip_bytes = HALF * STRIP * 4, TILES * D * 4
        ahi_sb = reuse("ahi_sb", stage_slots, [P, SPLITS, HALF, STRIP])
        alo_sb = reuse("alo_sb", stage_slots, [P, SPLITS, HALF, STRIP], at=SPLITS * half_bytes)
        ghi_first_sb = reuse("ghi_first_sb", first_digit_slots, [P, SPLIT_J, TILES, D])
        glo_first_sb = reuse("glo_first_sb", first_digit_slots, [P, SPLIT_J, TILES, D], at=SPLIT_J * strip_bytes)
        ghi_late_sb = reuse("ghi_late_sb", digit_slots, [P, NS - LATE_J, TILES, D])
        glo_late_sb = reuse("glo_late_sb", digit_slots, [P, NS - LATE_J, TILES, D], at=(NS - LATE_J) * strip_bytes)

        def ghi(again, j):
            return ghi_late_sb[:, j - LATE_J] if again else ghi_first_sb[:, j]

        def glo(again, j):
            return glo_late_sb[:, j - LATE_J] if again else glo_first_sb[:, j]

        h_ps = [ctx.enter_context(nc.psum_tensor(f"h_ps{k}", [P, STRIP], F32)) for k in range(BANKS)]
        rows_ps = ctx.enter_context(nc.psum_tensor("rows_ps", [P, 512], F32))
        y_ps = ctx.enter_context(nc.psum_tensor("y_ps", [P, TILES, D], F32))

        block_loaded = [sem(f"block_loaded{k}") for k in range(SLOTS + len(guest_slots))]
        x_loaded = [sem(f"x_loaded{s}") for s in range(NS)]
        xres_loaded = [sem(f"xres_loaded{k}") for k in range(2)]
        stored = [sem(f"stored{k}") for k in range(2)]
        weights_loaded = sem("weights_loaded")
        bias_loaded = sem("bias_loaded")
        ident_zeroed = sem("ident_zeroed")
        ident_ready = sem("ident_ready")
        ones_ready = sem("ones_ready")
        power_ready = sem("power_ready")
        ln_summed = sem("ln_summed")
        ln_squared = sem("ln_squared")
        h_ready = sem("h_ready")
        ln_centred = sem("ln_centred")
        ln_var = sem("ln_var")
        ln_rstd = sem("ln_rstd")
        ln_scale = sem("ln_scale")
        diagonal_added = sem("diagonal_added")
        sums_done = sem("sums_done")
        halves_done = sem("halves_done")
        folded = sem("folded")
        rows_summed = sem("rows_summed")
        rows_copied = sem("rows_copied")
        dinv_ready = sem("dinv_ready")
        g_ready = sem("g_ready")
        products_done = sem("products_done")
        ghi_ready = sem("ghi_ready")
        glo_ready = sem("glo_ready")
        ahi_ready = sem("ahi_ready")
        alo_ready = sem("alo_ready")
        halves_multiplied = sem("halves_multiplied")
        parts_taken = sem("parts_taken")
        wholes_taken = sem("wholes_taken")
        outputs_done = sem("outputs_done")
        outputs_scaled = sem("outputs_scaled")
        xres_biased = sem("xres_biased")
        residual_added = sem("residual_added")

        def wait_multiplied(engine, n):
            if n in split_half:
                engine.wait_ge(halves_multiplied, split_half[n])
            else:
                engine.wait_ge(products_done, product_step[n])

        def wait_slots_left(engine, slots):
            held = [n for n, slot in enumerate(slot_of) if slot in slots and not loads[n][2]]
            engine.wait_ge(sums_done, max(sum_step[n] for n in held))
            engine.wait_ge(products_done, max(product_step.get(n, 0) for n in held))
            if any(n in split_half for n in held):
                engine.wait_ge(alo_ready, max(split_half.get(n, 0) for n in held))

        block = ctx.enter_context(nc.Block())

        @block.sync
        def _(sp):
            def load_x(s):
                sp.dma_start(g_sb[:, s].rearrange("p a d -> p (a d)"), x_v[s]).then_inc(x_loaded[s], 16)

            def wait_left(old):
                if old < FIRST_PASS:
                    sp.wait_ge(sums_done, sum_step[old])
                if old in split_half:
                    sp.wait_ge(alo_ready, split_half[old])
                elif old in product_step:
                    sp.wait_ge(products_done, product_step[old])

            load_x(0)
            for n, (i, j, again) in enumerate(loads):
                if held_before[n] is not None:
                    wait_left(held_before[n])
                sp.dma_start(slot_ap(slot_of[n]), adj[i, j]).then_inc(block_loaded[slot_of[n]], 16)
                if n == 1:
                    sp.dma_start(wT_sb[:], wT).then_inc(weights_loaded, 16)
                if n % NS == X_AT and n // NS + 1 < NS and n < FIRST_PASS:
                    for k, (buffer, first, _) in enumerate(guest_slots):
                        if (buffer, first) == ("g", n // NS + 1):
                            wait_left(max(m for m, slot in enumerate(slot_of) if slot == SLOTS + k))
                    load_x(n // NS + 1)

        @block.vector
        def _(dve):
            nc.vector.memset(ones_sb[:], 1.0).then_inc(ones_ready, 1)

            def split_low(n):
                _, j, again = loads[n]
                if n == split[0]:
                    wait_slots_left(dve, stage_slots)
                    wait_slots_left(dve, first_digit_slots)
                if n == first_late:
                    dve.wait_ge(halves_multiplied, split_half[n] - 2)
                    wait_slots_left(dve, digit_slots)
                if n == min(m for m in split if loads[m][1:] == (j, again)):
                    dve.wait_ge(ghi_ready, digits.index((again, j)) + 1)
                    nc.vector.tensor_tensor(glo(again, j), g_sb[:, j], ghi(again, j), ALU.subtract).then_inc(glo_ready, 1)
                for half in range(2):
                    k = split_half[n] - 2 + half
                    dve.wait_ge(ahi_ready, k + 1)
                    if k >= SPLITS:
                        dve.wait_ge(halves_multiplied, k - SPLITS + 1)
                    nc.vector.tensor_tensor(alo_sb[:, k % SPLITS],
                                            slot_ap(slot_of[n])[:, half * HALF:(half + 1) * HALF],
                                            ahi_sb[:, k % SPLITS], ALU.subtract).then_inc(alo_ready, 1)

            def splits_after(n):
                for m in split_after.get(n, []):
                    split_low(m)

            for s in range(NS):
                for k in range(NS):
                    n = s * NS + k
                    tile = slot_ap(slot_of[n])
                    dve.wait_ge(block_loaded[slot_of[n]], 16 * fill[n])
                    if loads[n][0] == loads[n][1]:
                        if s == 0:
                            dve.wait_ge(ident_ready, 1)
                        diagonal = tile.rearrange("p a (c q) -> p (a c) q", q=P)[:, 0:TILES * TILES:TILES + 1]
                        nc.vector.tensor_tensor(diagonal, diagonal, ident_sb[:, None, :].to_broadcast([P, TILES, P]),
                                                ALU.add).then_inc(diagonal_added, 1)
                        dve.wait_ge(diagonal_added, s + 1)
                    flat = tile.rearrange("p a i -> p (a i)")
                    if k == 0:
                        splits_after(n)
                        continue
                    if k == 1:
                        before = slot_ap(slot_of[n - 1]).rearrange("p a i -> p (a i)")
                        if s > 0:
                            dve.wait_ge(folded, s)
                    else:
                        before = acc_sb[:]
                        dve.wait_ge(sums_done, sum_step[n] - 1)
                    nc.vector.tensor_tensor(acc_sb[:], before, flat, ALU.add).then_inc(sums_done, 1)
                    if k < NS - 1:
                        splits_after(n)
                dve.wait_ge(sums_done, (s + 1) * (NS - 1))
                nc.vector.tensor_tensor(acc_sb[:, 0:2 * STRIP], acc_sb[:, 0:2 * STRIP], acc_sb[:, 2 * STRIP:4 * STRIP],
                                        ALU.add).then_inc(halves_done, 1)
                dve.wait_ge(halves_done, s + 1)
                if s >= 2:
                    dve.wait_ge(rows_summed, s - 1)
                nc.vector.tensor_tensor(fold_sb[:, s % 2], acc_sb[:, 0:STRIP], acc_sb[:, STRIP:2 * STRIP],
                                        ALU.add).then_inc(folded, 1)
                splits_after((s + 1) * NS - 1)
            for kind, what in late_steps(DVE_LATER):
                if kind == "block":
                    if what[1] in split_half:
                        split_low(what[1])
                elif what >= DIRECT:
                    e, group = what, NS + what - DIRECT
                    wait_multiplied(dve, group_end[group])
                    dve.wait_ge(parts_taken, order[e - DIRECT] + 1)
                    dve.wait_ge(outputs_done, e - 1)
                    nc.vector.tensor_tensor(ht_sb[:, e % 2], h_ps[group % BANKS][:], part_sb[:, order[e - DIRECT]],
                                            ALU.add).then_inc(wholes_taken, 1)

        @block.tensor
        def _(pe):
            pe.wait_ge(ones_ready, 1)

            def row_sums(s):
                pe.wait_ge(folded, s + 1)
                if s >= 1:
                    pe.wait_ge(rows_copied, s)
                for a in range(TILES):
                    last = nc.tensor.matmul(rows_ps[:, a:a + 1], fold_sb[:, s % 2, a * P:(a + 1) * P], ones_sb[:],
                                            start=True, stop=True)
                last.then_inc(rows_summed, 1)

            def product(n, group, first, last_of_group):
                i, j, again = loads[n]
                if n not in split_half:
                    pe.wait_ge(block_loaded[slot_of[n]], 16 * fill[n])
                if i == j:
                    pe.wait_ge(diagonal_added, i + 1)
                pe.wait_ge(g_ready, j + 1)
                if first and group >= BANKS:
                    old = group - BANKS
                    if old < NS:
                        pe.wait_ge(parts_taken, old + 1)
                    else:
                        pe.wait_ge(wholes_taken, old - NS + 1)
                bank = h_ps[group % BANKS]
                for a in range(TILES):
                    start, stop = first and a == 0, last_of_group and a == TILES - 1
                    if n not in split_half:
                        mm = nc.tensor.matmul(bank[:], g_sb[:, j, a], slot_ap(slot_of[n])[:, a], start=start, stop=stop)
                        continue
                    k = split_half[n] - 2 + a // HALF
                    pe.wait_ge(glo_ready, digits.index((again, j)) + 1)
                    pe.wait_ge(ahi_ready, k + 1)
                    ahi, alo = ahi_sb[:, k % SPLITS, a % HALF], alo_sb[:, k % SPLITS, a % HALF]
                    nc.tensor.matmul(bank[:], ghi(again, j)[:, a], ahi, start=start, stop=False)
                    nc.tensor.matmul(bank[:], glo(again, j)[:, a], ahi, start=False, stop=False)
                    pe.wait_ge(alo_ready, k + 1)
                    mm = nc.tensor.matmul(bank[:], ghi(again, j)[:, a], alo, start=False, stop=stop)
                    if a % HALF == HALF - 1:
                        mm.then_inc(halves_multiplied, 1)
                if n not in split_half:
                    mm.then_inc(products_done, 1)

            def output(e):
                if e == 0:
                    pe.wait_ge(weights_loaded, 16)
                if e < DIRECT:
                    pe.wait_ge(parts_taken, RETAKEN + e + 1)
                else:
                    pe.wait_ge(wholes_taken, e - DIRECT + 1)
                if e >= 1:
                    pe.wait_ge(outputs_scaled, e)
                for a in range(TILES):
                    mm = nc.tensor.matmul(y_ps[:, a], ht_sb[:, e % 2, a * P:(a + 1) * P], wT_sb[:],
                                          start=True, stop=True)
                mm.then_inc(outputs_done, 1)

            for step in steps:
                if step[0] == "row sums":
                    row_sums(step[1])
                elif not loads[step[1]][2]:
                    product(*step[1:])
            for kind, what in late_steps(PE_LATER):
                if kind == "block":
                    product(*what[1:])
                else:
                    output(what)

        strip_of_output = list(range(RETAKEN, NS)) + order

        @block.scalar
        def _(act):
            def layernorm_relu(s):
                act.wait_ge(x_loaded[s], 16)
                for a in range(TILES):
                    if s + a > 0:
                        act.wait_ge(ln_summed, s * TILES + a)
                    nc.scalar.activation(scratch_sb[:], g_sb[:, s, a], ACT.Copy,
                                         accum_out=sum_sb[:, s % 2, a:a + 1]).then_inc(ln_summed, 1)
                act.wait_ge(ln_summed, (s + 1) * TILES)
                act.wait_ge(ln_centred, s + 1)
                for a in range(TILES):
                    if s + a > 0:
                        act.wait_ge(ln_squared, s * TILES + a)
                    nc.scalar.activation(scratch_sb[:], g_sb[:, s, a], ACT.Square, bias=negmean_sb[:, s % 2, a:a + 1],
                                         accum_out=square_sb[:, s % 2, a:a + 1]).then_inc(ln_squared, 1)
                act.wait_ge(ln_squared, (s + 1) * TILES)
                act.wait_ge(ln_scale, s + 1)
                for a in range(TILES):
                    nc.scalar.activation(g_sb[:, s, a], g_sb[:, s, a], ACT.Relu, bias=shift_sb[:, s % 2, a:a + 1],
                                         scale=rstd_sb[:, s % 2, a:a + 1]).then_inc(h_ready, 1)

            def take_part(group):
                wait_multiplied(act, group_end[group])
                if group < RETAKEN:
                    dst = part_sb[:, group]
                else:
                    e = group - RETAKEN
                    if e >= 2:
                        act.wait_ge(outputs_done, e - 1)
                    dst = ht_sb[:, e % 2]
                nc.scalar.activation(dst, h_ps[group % BANKS][:], ACT.Copy).then_inc(parts_taken, 1)

            def scale_output(e):
                act.wait_ge(outputs_done, e + 1)
                if e == 0:
                    act.wait_ge(folded, NS)
                if e >= 2:
                    act.wait_ge(stored[e % 2], 16 * (e // 2))
                for a in range(TILES):
                    ins = nc.scalar.activation(y_sb[:, e % 2, a], y_ps[:, a], ACT.Copy,
                                               scale=dinv_sb[:, strip_of_output[e], a:a + 1])
                ins.then_inc(outputs_scaled, 1)

            def split_high(n):
                _, j, again = loads[n]
                if n == split[0]:
                    wait_slots_left(act, stage_slots)
                    wait_slots_left(act, first_digit_slots)
                if n == first_late:
                    act.wait_ge(halves_multiplied, split_half[n] - 2)
                    wait_slots_left(act, digit_slots)
                if n == min(m for m in split if loads[m][1:] == (j, again)):
                    act.wait_ge(g_ready, j + 1)
                    nc.scalar.activation(ghi(again, j), g_sb[:, j], ACT.Copy).then_inc(ghi_ready, 1)
                act.wait_ge(block_loaded[slot_of[n]], 16 * fill[n])
                for half in range(2):
                    k = split_half[n] - 2 + half
                    if k >= SPLITS:
                        act.wait_ge(halves_multiplied, k - SPLITS + 1)
                        act.wait_ge(alo_ready, k - SPLITS + 1)
                    nc.scalar.activation(ahi_sb[:, k % SPLITS], slot_ap(slot_of[n])[:, half * HALF:(half + 1) * HALF],
                                         ACT.Copy).then_inc(ahi_ready, 1)

            layernorm_relu(0)
            for s in range(NS):
                if s + 1 < NS:
                    layernorm_relu(s + 1)
                for n in split:
                    if loads[n][0] == s and not loads[n][2]:
                        split_high(n)
                act.wait_ge(rows_summed, s + 1)
                nc.scalar.activation(rows_sb[:, s], rows_ps[:, 0:TILES], ACT.Copy).then_inc(rows_copied, 1)
                act.wait_ge(dinv_ready, s + 1)
                act.wait_ge(h_ready, (s + 1) * TILES)
                for a in range(TILES):
                    ins = nc.scalar.activation(g_sb[:, s, a], g_sb[:, s, a], ACT.Copy, scale=dinv_sb[:, s, a:a + 1])
                ins.then_inc(g_ready, 1)
                for i in range(RETAKEN + 1):
                    if reach(i, NS) == s:
                        take_part(i)
            take_part(RETAKEN + 1)
            for kind, what in late_steps(ACT_LATER):
                if kind == "block":
                    if what[1] in split_half:
                        split_high(what[1])
                else:
                    scale_output(what)
                    if RETAKEN + what + 2 < NS:
                        take_part(RETAKEN + what + 2)

        @block.gpsimd
        def _(pool):
            nc.gpsimd.memset(ident_sb[:], 0.0).then_inc(ident_zeroed, 1)
            nc.gpsimd.memset(power_sb[:], -0.5).then_inc(power_ready, 1)
            pool.wait_ge(ident_zeroed, 1)
            nc.gpsimd.affine_select(out=ident_sb[:], in_=ident_sb[:], compare_op=ALU.not_equal, fill=1.0, base=0,
                                    pattern=[[-1, P]], channel_multiplier=1).then_inc(ident_ready, 1)
            pool.dma_start(bias_sb[:], b[0:1, :].to_broadcast([P, D])).then_inc(bias_loaded, 16)
            pool.wait_ge(power_ready, 1)

            def layernorm_scale(s):
                pool.wait_ge(ln_summed, (s + 1) * TILES)
                nc.gpsimd.tensor_scalar(negmean_sb[:, s % 2], sum_sb[:, s % 2], -1.0 / D, None, ALU.mult).then_inc(ln_centred, 1)
                pool.wait_ge(ln_squared, (s + 1) * TILES)
                nc.gpsimd.tensor_scalar(var_sb[:, s % 2], square_sb[:, s % 2], 1.0 / D, EPS, ALU.mult, ALU.add).then_inc(ln_var, 1)
                pool.wait_ge(ln_var, s + 1)
                nc.gpsimd.tensor_tensor(rstd_sb[:, s % 2], var_sb[:, s % 2], power_sb[:], ALU.pow).then_inc(ln_rstd, 1)
                pool.wait_ge(ln_rstd, s + 1)
                pool.wait_ge(ln_centred, s + 1)
                nc.gpsimd.tensor_tensor(shift_sb[:, s % 2], negmean_sb[:, s % 2], rstd_sb[:, s % 2], ALU.mult).then_inc(ln_scale, 1)

            layernorm_scale(0)
            for s in range(NS):
                if s + 1 < NS:
                    layernorm_scale(s + 1)
                pool.wait_ge(rows_copied, s + 1)
                nc.gpsimd.tensor_tensor(dinv_sb[:, s], rows_sb[:, s], power_sb[:], ALU.pow).then_inc(dinv_ready, 1)

            def load_residual(e):
                pool.dma_start(xres_sb[:, e % 2].rearrange("p a d -> p (a d)"), x_v[strip_of_output[e]])\
                    .then_inc(xres_loaded[e % 2], 16)

            pool.wait_ge(bias_loaded, 16)
            pool.wait_ge(folded, NS)
            load_residual(0)
            for e in range(NS):
                if e >= 1:
                    pool.wait_ge(residual_added, e)
                if e + 1 < NS:
                    load_residual(e + 1)
                pool.wait_ge(xres_loaded[e % 2], 16 * (e // 2 + 1))
                nc.gpsimd.tensor_tensor(xres_sb[:, e % 2], xres_sb[:, e % 2],
                                        bias_sb[:, None, :].to_broadcast([P, TILES, D]), ALU.add)\
                    .then_inc(xres_biased, 1)
                pool.wait_ge(xres_biased, e + 1)
                pool.wait_ge(outputs_scaled, e + 1)
                nc.gpsimd.tensor_tensor(y_sb[:, e % 2], y_sb[:, e % 2], xres_sb[:, e % 2], ALU.add)\
                    .then_inc(residual_added, 1)
                pool.wait_ge(residual_added, e + 1)
                pool.dma_start(out_v[strip_of_output[e]], y_sb[:, e % 2].rearrange("p a d -> p (a d)"))\
                    .then_inc(stored[e % 2], 16)
            for k in range(2):
                pool.wait_ge(stored[k], 16 * (NS // 2))


def kernel(x, adj, L0_gnn_W, L0_gnn_b):
    import numpy as np
    import concourse.bacc as bacc
    from concourse.bass_utils import run_bass_kernel_spmd

    n = x.shape[0]
    s = n // STRIP
    blocks = np.asarray(adj).reshape(s, P, TILES, s, P, TILES).transpose(0, 3, 4, 5, 2, 1)
    arrays = {
        "x": np.ascontiguousarray(x),
        "adj": np.ascontiguousarray(blocks).reshape(s, s, P, TILES, STRIP),
        "wT": np.ascontiguousarray(np.asarray(L0_gnn_W).T),
        "b": np.ascontiguousarray(L0_gnn_b).reshape(1, D),
    }
    nc = bacc.Bacc("TRN2", target_bir_lowering=False, num_devices=1)
    args = [nc.dram_tensor(k, v.shape, mybir.dt.from_np(v.dtype), kind="ExternalInput").ap() for k, v in arrays.items()]
    out = nc.dram_tensor("out", (n, D), mybir.dt.float32, kind="ExternalOutput").ap()
    preln_gcn_kernel(nc, *args, out)
    r = run_bass_kernel_spmd(nc, [arrays], core_ids=[0])
    return r.results[0]["out"]
```
